# Optimizing a Trainium2 kernel written in Bass

```python
import numpy as np
import jax
import jax.numpy as jnp

def _softmax(x, axis=-1):
    return jax.nn.softmax(x, axis=axis)
def _gelu(x):
    return jax.nn.gelu(x, approximate=True)
def _silu(x):
    return jax.nn.silu(x)
def _sigmoid(x):
    return jax.nn.sigmoid(x)
def _layernorm(x, axis=-1, eps=1e-5):
    m = jnp.mean(x, axis=axis, keepdims=True)
    v = jnp.var(x, axis=axis, keepdims=True)
    return (x - m) / jnp.sqrt(v + eps)
def _scatter_add(tgt, idx, src, axis=0):
    return tgt.at[idx].add(src)
def _segment_sum(src, seg, n):
    return jax.ops.segment_sum(src, seg, n)

kernel_name = 'mk_rec_standalone_d1_rec_acb1f1'

def setup_inputs(seed: int = 0):
    np.random.seed(seed)
    _w = jnp.asarray
    def _rec_inputs():
        import jax
        import jax.numpy as jnp
        _rk = jax.random.key(seed)
        r_input_emb = -7.10856e-05 + 0.999911 * jax.random.normal(jax.random.fold_in(_rk, 1), (16384, 64, 64), jnp.float32)
        return r_input_emb
    r_input_emb = _rec_inputs()
    def _L0_rec_setup():
        import jax, jax.numpy as jnp
        import numpy as np
        EPS = 1e-08

        def _split_heads(x, H):
            B, F, E = x.shape
            return x.reshape(B, F, H, E // H).transpose(2, 0, 1, 3)
        key = jax.random.key(seed)
        ks = jax.random.split(key, 6)
        B, F, E = (16384, 64, 64)
        s = 1.0 / np.sqrt(E)
        return {'input_emb': jax.random.normal(ks[0], (B, F, E), jnp.float32), 'QW': jax.random.normal(ks[1], (E, E), jnp.float32) * s, 'Qb': jnp.zeros((E,), jnp.float32), 'KW': jax.random.normal(ks[2], (E, E), jnp.float32) * s, 'Kb': jnp.zeros((E,), jnp.float32), 'VW': jax.random.normal(ks[3], (E, E), jnp.float32) * s, 'Vb': jnp.zeros((E,), jnp.float32), 'RW': jax.random.normal(ks[4], (E, E), jnp.float32) * s, 'Rb': jnp.zeros((E,), jnp.float32), 'gamma': jnp.ones((E,), jnp.float32), 'beta': jnp.zeros((E,), jnp.float32), 'num_head': 2}
    _L0_rec_all = _L0_rec_setup()
    _L0_rec_in = {k: v for k, v in _L0_rec_all.items() if k in ('QW', 'Qb', 'KW', 'Kb', 'VW', 'Vb', 'RW', 'Rb', 'gamma', 'beta', )}
    del _L0_rec_all

    return {
        "r_input_emb": r_input_emb,
        "L0_rec_QW": _L0_rec_in["QW"],
        "L0_rec_Qb": _L0_rec_in["Qb"],
        "L0_rec_KW": _L0_rec_in["KW"],
        "L0_rec_Kb": _L0_rec_in["Kb"],
        "L0_rec_VW": _L0_rec_in["VW"],
        "L0_rec_Vb": _L0_rec_in["Vb"],
        "L0_rec_RW": _L0_rec_in["RW"],
        "L0_rec_Rb": _L0_rec_in["Rb"],
        "L0_rec_gamma": _L0_rec_in["gamma"],
        "L0_rec_beta": _L0_rec_in["beta"],
    }

def reference(r_input_emb, L0_rec_QW, L0_rec_Qb, L0_rec_KW, L0_rec_Kb, L0_rec_VW, L0_rec_Vb, L0_rec_RW, L0_rec_Rb, L0_rec_gamma, L0_rec_beta):
    import jax
    import jax.numpy as jnp
    def _L0_rec_ref(input_emb, QW, Qb, KW, Kb, VW, Vb, RW, Rb, gamma, beta, num_head):
        import jax, jax.numpy as jnp
        import numpy as np
        EPS = 1e-08

        def _split_heads(x, H):
            B, F, E = x.shape
            return x.reshape(B, F, H, E // H).transpose(2, 0, 1, 3)
        relu = jax.nn.relu
        H = num_head
        B, F, E = input_emb.shape
        dh = E // H
        Q = _split_heads(relu(input_emb @ QW + Qb), H)
        K = _split_heads(relu(input_emb @ KW + Kb), H)
        V = _split_heads(relu(input_emb @ VW + Vb), H)
        w = jnp.einsum('hbqd,hbkd->hbqk', Q, K) / jnp.sqrt(jnp.float32(dh))
        w = jax.nn.softmax(w, axis=-1)
        out = jnp.einsum('hbqk,hbkd->hbqd', w, V)
        out = out.transpose(1, 2, 0, 3).reshape(B, F, E)
        out = out + relu(input_emb @ RW + Rb)
        out = relu(out)
        mean = jnp.mean(out, axis=-1, keepdims=True)
        var = jnp.mean((out - mean) ** 2, axis=-1, keepdims=True)
        normed = (out - mean) / jnp.sqrt(var + EPS)
        return gamma * normed + beta

    y = _L0_rec_ref(r_input_emb, L0_rec_QW, L0_rec_Qb, L0_rec_KW, L0_rec_Kb, L0_rec_VW, L0_rec_Vb, L0_rec_RW, L0_rec_Rb, L0_rec_gamma, L0_rec_beta, 2)
    return y


_drawn_inputs = setup_inputs


def setup_inputs(seed=0):
    import zlib

    import numpy as np

    out = dict(_drawn_inputs(seed))
    spreads = {'L0_rec_Qb': (0.0, 0.8),
     'L0_rec_Kb': (0.0, 0.8),
     'L0_rec_Vb': (0.0, 0.1),
     'L0_rec_Rb': (0.0, 0.1),
     'L0_rec_gamma': (1.0, 0.2),
     'L0_rec_beta': (0.0, 0.1)}
    factors = {}
    for name, (base, spread) in spreads.items():
        noise = np.random.default_rng([zlib.crc32(name.encode()), seed]).standard_normal(out[name].shape)
        drawn = base * np.exp(spread * noise) if base else spread * noise
        out[name] = jnp.asarray(drawn.astype(out[name].dtype))
    for name, factor in factors.items():
        out[name] = (out[name] * factor).astype(out[name].dtype)
    return out
```

```python
from contextlib import ExitStack

import concourse.bass as bass
from concourse import mybir

ALU = mybir.AluOpType
ACT = mybir.ActivationFunctionType
AX_X = mybir.AxisListType.X
BF16 = mybir.dt.bfloat16
F32 = mybir.dt.float32

P = 128
F = 64
E = 64
H = 2
DH = E // H
G = 2
T = 4
GT = G * T
COLS = T * P
CHUNK = G * COLS
NB = COLS // F
VW = DH + 1
EPS = 1e-08


def rec_attention(nc, x, qw, qb, kw, kb, vw, vb, rw, rb, gamma, beta, out):
    n_batch, _, _ = x.shape
    n_chunks = n_batch * F // CHUNK
    assert n_chunks * CHUNK == n_batch * F and n_chunks % 2 == 0 and n_chunks >= 4
    scale = float(DH) ** -0.5

    x_view = x.rearrange("b f e -> (b f) e").rearrange("(c g t p) e -> c g p t e", g=G, t=T, p=P)
    out_view = out.rearrange("b f e -> (b f) e").rearrange("(c n p) e -> c p n e", n=GT, p=P)

    with ExitStack() as ctx:
        def sb(name, shape, dt=F32):
            return ctx.enter_context(nc.sbuf_tensor(name, shape, dt))

        def bank(name, dt=F32):
            return ctx.enter_context(nc.psum_tensor(name, [P, 512 if dt == F32 else 1024], dt))

        def sem(name):
            return ctx.enter_context(nc.semaphore(name))

        ident = sb("ident", [P, P])
        ident_bf = sb("ident_bf", [P, P], BF16)
        wq = sb("wq", [P, P])
        wk = sb("wk", [P, P])
        wvr = sb("wvr", [P, G, 2 * E])
        head_mask = sb("head_mask", [P, H])
        q_bias = sb("q_bias", [P, 1])
        q_bias_masked = sb("q_bias_masked", [P, H])
        k_bias = sb("k_bias", [P, 1])
        vr_bias_in = sb("vr_bias_in", [1, 2 * E])
        vr_bias_f32 = sb("vr_bias_f32", [1, 4, 2 * E])
        vr_bias_rest = sb("vr_bias_rest", [1, 2, 4 * 2 * E])
        vr_bias_part = sb("vr_bias_part", [1, 2, 4 * 2 * E], BF16)
        vr_bias = sb("vr_bias", [P, 4 * 2 * E], BF16)
        bias_rows = sb("bias_rows", [P, P], BF16)
        max_select = sb("max_select", [P, COLS], BF16)
        eps_all = sb("eps_all", [P, GT])
        minus_half = sb("minus_half", [P, GT])
        gamma_all = sb("gamma_all", [P, E])
        beta_all = sb("beta_all", [P, E])

        x_in = [sb(f"x_in{i}", [P, T, G, E]) for i in range(2)]
        xt = sb("xt", [P, COLS])
        q_t = sb("q_t", [P, NB, H, F])
        k_t = sb("k_t", [P, COLS])
        vr = [sb(f"vr{i}", [P, T, G, 4, VW]) for i in range(2)]
        row_max = [sb(f"row_max{g}", [P, NB]) for g in range(G)]
        neg_max = [sb(f"neg_max{g}", [P, 2 * NB], BF16) for g in range(G)]
        neg_max_t = [sb(f"neg_max_t{g}", [P, P], BF16) for g in range(G)]
        probs = [sb(f"probs{g}", [P, COLS]) for g in range(G)]
        probs_t = [sb(f"probs_t{g}", [P, COLS]) for g in range(G)]
        recip = [sb(f"recip{g}", [P, T, H]) for g in range(G)]
        attn = [sb(f"attn{g}", [P, T, E]) for g in range(G)]
        y = [sb(f"y{i}", [P, GT, E]) for i in range(2)]
        stats = sb("stats", [P, GT, 6])
        moments = [sb(f"moments{i}", [P, GT, 2]) for i in range(2)]
        var_eps = sb("var_eps", [P, GT])
        rstd = sb("rstd", [P, GT])
        centred = sb("centred", [P, GT, E])
        normed = sb("normed", [P, GT, E])
        scaled = sb("scaled", [P, GT, E])
        y_out = [sb(f"y_out{i}", [P, GT, E]) for i in range(2)]

        front = [bank(f"front{i}") for i in range(2)]
        score = [bank(f"score{g}") for g in range(G)]
        turned = [bank(f"turned{g}") for g in range(G)]
        turned_bf = [t[:, :].bitcast(BF16) for t in turned]
        attn_ps = [bank(f"attn_ps{g}") for g in range(G)]

        const_loaded = sem("const_loaded")
        const_zeroed = sem("const_zeroed")
        const_made = sem("const_made")
        bias_step = sem("bias_step")
        x_loaded = [sem(f"x_loaded{i}") for i in range(2)]
        xt_ready = sem("xt_ready")
        xt_copied = sem("xt_copied")
        q_ready = sem("q_ready")
        q_copied = sem("q_copied")
        k_ready = sem("k_ready")
        k_copied = sem("k_copied")
        vr_ready = sem("vr_ready")
        vr_copied = sem("vr_copied")
        scores_ready = sem("scores_ready")
        max_found = sem("max_found")
        max_high = sem("max_high")
        max_split = sem("max_split")
        max_turned = sem("max_turned")
        max_t_copied = sem("max_t_copied")
        shifted_ready = sem("shifted_ready")
        exp_done = sem("exp_done")
        probs_turned = sem("probs_turned")
        probs_t_copied = sem("probs_t_copied")
        attn_ready = sem("attn_ready")
        recip_done = sem("recip_done")
        attn_normed = sem("attn_normed")
        y_added = sem("y_added")
        stats_done = sem("stats_done")
        moments_done = sem("moments_done")
        var_eps_done = sem("var_eps_done")
        rstd_done = sem("rstd_done")
        centred_done = sem("centred_done")
        normed_done = sem("normed_done")
        scaled_done = sem("scaled_done")
        result_done = sem("result_done")
        stored = [sem(f"stored{i}") for i in range(2)]

        N_CONST_DMAS = 6 * G + 4
        block = ctx.enter_context(nc.Block())

        @block.sync
        def _(sp):
            sp.wait_ge(const_zeroed, 1)
            n = 0
            for g in range(G):
                r = slice(g * E, (g + 1) * E)
                for dst, src in (
                    (wq[r, r], qw), (wk[r, r], kw), (wvr[r, g, 0:E], vw), (wvr[r, g, E:2 * E], rw),
                    (q_bias[r, :], qb.rearrange("(e o) -> e o", o=1)),
                    (k_bias[r, :], kb.rearrange("(e o) -> e o", o=1)),
                ):
                    sp.dma_start(dst, src).then_inc(const_loaded, 16)
                    n += 1
            sp.dma_start(vr_bias_in[:, 0:E], vb.rearrange("(o e) -> o e", o=1)).then_inc(const_loaded, 16)
            sp.dma_start(vr_bias_in[:, E:2 * E], rb.rearrange("(o e) -> o e", o=1)).then_inc(const_loaded, 16)
            sp.dma_start(gamma_all[:, :], gamma.partition_broadcast(P)).then_inc(const_loaded, 16)
            sp.dma_start(beta_all[:, :], beta.partition_broadcast(P)).then_inc(const_loaded, 16)
            assert n + 4 == N_CONST_DMAS

            def load(c, slot):
                for g in range(G):
                    sp.dma_start(x_in[slot][:, :, g, :], x_view[c, g]).then_inc(x_loaded[slot], 16)

            def store(c, slot):
                sp.wait_ge(result_done, c + 1)
                sp.dma_start(out_view[c], y_out[slot][:, :, :]).then_inc(stored[slot], 16)

            load(0, 0)
            load(1, 1)
            sp.wait_ge(xt_ready, 1)
            load(2, 0)
            sp.wait_ge(xt_ready, 2)
            load(3, 1)
            with sp.Fori(0, n_chunks // 2 - 2) as pair:
                c = 2 * pair
                for k in range(2):
                    sp.wait_ge(xt_ready, c + k + 3)
                    load(c + k + 4, k)
                    store(c + k, k)
            for c in range(n_chunks - 4, n_chunks):
                store(c, c % 2)
            for k in range(2):
                sp.wait_ge(stored[k], 16 * (n_chunks // 2))

        @block.gpsimd
        def _(pool):
            for m in (wq, wk, wvr, ident, ident_bf, vr_bias, bias_rows, max_select, neg_max_t[0], neg_max_t[1]):
                flat = m[:, :, :] if m is wvr else m[:, :]
                last = nc.gpsimd.memset(flat, 0.0)
            last.then_inc(const_zeroed, 1)
            pool.wait_ge(const_zeroed, 1)
            for m in (ident, ident_bf):
                nc.gpsimd.affine_select(out=m[:, :], in_=m[:, :], compare_op=ALU.not_equal, fill=1.0, base=0,
                                        pattern=[[-1, P]], channel_multiplier=1)
            sel = max_select[:, :].rearrange("p (j k) -> p j k", j=NB)
            for part in range(2):
                last = nc.gpsimd.affine_select(out=sel, in_=sel, compare_op=ALU.not_equal, fill=1.0,
                                               base=-part * NB, pattern=[[-1, NB], [0, F]], channel_multiplier=1)
                last.then_inc(const_zeroed, 1)
                pool.wait_ge(const_zeroed, 2 + part)
            for row in (0, 32, 64):
                nc.gpsimd.memset(bias_rows[row:row + 1, :], 1.0)
            for q in range(4):
                for h in range(H):
                    last = nc.gpsimd.memset(head_mask[q * DH:(q + 1) * DH, h:h + 1], 1.0 if q % H == h else 0.0)
            last.then_inc(const_zeroed, 1)
            pool.wait_ge(const_zeroed, 4)
            nc.gpsimd.memset(eps_all[:, :], EPS)
            nc.gpsimd.memset(minus_half[:, :], -0.5)
            for i in range(2):
                last = nc.gpsimd.memset(vr[i][:, :, :, :, :], 1.0)
            last.then_inc(const_made, 1)
            pool.wait_ge(const_loaded, 16 * (N_CONST_DMAS))

            def finish(c, slot):
                whole = [P, GT, E]
                mean = moments[slot][:, :, 0:1].to_broadcast(whole)
                pool.wait_ge(moments_done, c + 1)
                pool.tensor_tensor(var_eps[:, :].unsqueeze(2), moments[slot][:, :, 1:2],
                                   eps_all[:, :].unsqueeze(2), ALU.add).then_inc(var_eps_done, 1)
                pool.wait_ge(var_eps_done, c + 1)
                pool.tensor_tensor(rstd[:, :], var_eps[:, :], minus_half[:, :], ALU.pow).then_inc(rstd_done, 1)
                pool.tensor_tensor(centred[:, :, :], y[slot][:, :, :], mean, ALU.subtract).then_inc(centred_done, 1)
                pool.wait_ge(centred_done, c + 1)
                pool.wait_ge(rstd_done, c + 1)
                pool.tensor_tensor(normed[:, :, :], centred[:, :, :],
                                   rstd[:, :].unsqueeze(2).to_broadcast(whole),
                                   ALU.mult).then_inc(normed_done, 1)
                pool.wait_ge(normed_done, c + 1)
                pool.tensor_tensor(scaled[:, :, :], normed[:, :, :],
                                   gamma_all[:, :].unsqueeze(1).to_broadcast(whole),
                                   ALU.mult).then_inc(scaled_done, 1)
                pool.wait_ge(scaled_done, c + 1)

            def add_beta(c, slot):
                pool.tensor_tensor(y_out[slot][:, :, :], scaled[:, :, :],
                                   beta_all[:, :].unsqueeze(1).to_broadcast([P, GT, E]),
                                   ALU.add).then_inc(result_done, 1)

            for c in range(2):
                finish(c, c)
                add_beta(c, c)
            with pool.Fori(1, n_chunks // 2) as pair:
                for k in range(2):
                    finish(2 * pair + k, k)
                    pool.wait_ge(stored[k], 16 * pair)
                    add_beta(2 * pair + k, k)

        @block.scalar
        def _(act):
            act.wait_ge(const_made, 2)

            def copy_xt(c, par):
                act.wait_ge(xt_ready, c + 1)
                nc.scalar.activation(xt[:, :], front[par][:, :], ACT.Copy).then_inc(xt_copied, 1)

            def relu_q(c, par):
                act.wait_ge(q_ready, c + 1)
                for h in range(H):
                    last = nc.scalar.activation(
                        q_t[:, :, h, :], front[1 - par][:, :].rearrange("k (n q) -> k n q", n=NB), ACT.Relu,
                        bias=q_bias_masked[:, h:h + 1], scale=head_mask[:, h:h + 1])
                last.then_inc(q_copied, 1)

            def relu_k(c, par):
                act.wait_ge(k_ready, c + 1)
                nc.scalar.activation(k_t[:, :], front[par][:, :], ACT.Relu,
                                     bias=k_bias[:, 0:1]).then_inc(k_copied, 1)

            def relu_vr(c, u, par):
                act.wait_ge(vr_ready, 2 * c + u + 1)
                nc.scalar.activation(
                    vr[par][:, 2 * u:2 * u + 2, :, :, 0:DH],
                    front[(par + 3 + u) % 2][:, :].rearrange("p (t g b d) -> p t g b d", t=2, g=G, b=4),
                    ACT.Relu).then_inc(vr_copied, 1)

            def exps(c, g):
                act.wait_ge(shifted_ready, 2 * c + g + 1)
                nc.scalar.activation(probs[g][:, :], score[g][:, :], ACT.Exp, scale=scale).then_inc(exp_done, 1)

            def copy_probs_t(c, g):
                act.wait_ge(probs_turned, 2 * c + g + 1)
                nc.scalar.activation(probs_t[g][:, :], turned[g][:, :], ACT.Copy).then_inc(probs_t_copied, 1)

            def step(c, par, first=False, last=False):
                if not last:
                    copy_xt(c + 1, 1 - par)
                exps(c, 0)
                if not last:
                    relu_q(c + 1, 1 - par)
                exps(c, 1)
                copy_probs_t(c, 0)
                if not last:
                    relu_k(c + 1, 1 - par)
                copy_probs_t(c, 1)
                if not last:
                    if not first:
                        act.wait_ge(attn_ready, 2 * c)
                        act.wait_ge(y_added, 2 * c)
                    relu_vr(c + 1, 0, 1 - par)
                    relu_vr(c + 1, 1, 1 - par)

            copy_xt(0, 0)
            relu_q(0, 0)
            relu_k(0, 0)
            relu_vr(0, 0, 0)
            relu_vr(0, 1, 0)
            step(0, 0, first=True)
            with act.Fori(0, n_chunks // 2 - 1) as pair:
                step(2 * pair + 1, 1)
                step(2 * pair + 2, 0)
            step(n_chunks - 1, 1, last=True)

        @block.vector
        def _(dve):
            dve.wait_ge(const_loaded, 16 * (N_CONST_DMAS))
            dve.wait_ge(const_made, 1)
            nc.vector.tensor_scalar(q_bias_masked[:, :], head_mask[:, :], q_bias[:, 0:1], None, ALU.mult)
            nc.vector.tensor_copy(vr_bias_f32[:, :, :],
                                  vr_bias_in[:, :].unsqueeze(1).to_broadcast([1, 4, 2 * E])).then_inc(bias_step, 1)
            dve.wait_ge(bias_step, 1)
            flat = vr_bias_f32[:, :, :].rearrange("o n e -> o (n e)")
            nc.vector.tensor_copy(vr_bias_part[:, 0, :], flat).then_inc(bias_step, 1)
            dve.wait_ge(bias_step, 2)
            nc.vector.tensor_tensor(vr_bias_rest[:, 0, :], flat, vr_bias_part[:, 0, :], ALU.subtract).then_inc(bias_step, 1)
            dve.wait_ge(bias_step, 3)
            nc.vector.tensor_copy(vr_bias_part[:, 1, :], vr_bias_rest[:, 0, :]).then_inc(bias_step, 1)
            dve.wait_ge(bias_step, 4)
            nc.vector.tensor_tensor(vr_bias_rest[:, 1, :], vr_bias_rest[:, 0, :], vr_bias_part[:, 1, :],
                                    ALU.subtract).then_inc(bias_step, 1)
            dve.wait_ge(bias_step, 5)
            nc.vector.tensor_copy(vr_bias[0:1, :], vr_bias_part[:, 0, :])
            nc.vector.tensor_copy(vr_bias[32:33, :], vr_bias_part[:, 1, :])
            nc.vector.tensor_copy(vr_bias[64:65, :], vr_bias_rest[:, 1, :]).then_inc(const_made, 1)

            def maxima(c, g):
                n = 2 * c + g + 1
                dve.wait_ge(scores_ready, n)
                nc.vector.tensor_reduce(row_max[g][:, :], score[g][:, :].rearrange("p (n k) -> p n k", n=NB),
                                        AX_X, ALU.max).then_inc(max_found, 1)
                dve.wait_ge(max_found, n)
                nc.vector.tensor_scalar(neg_max[g][:, 0:NB], row_max[g][:, :], -1.0, None,
                                        ALU.mult).then_inc(max_high, 1)
                dve.wait_ge(max_high, n)
                nc.vector.scalar_tensor_tensor(out=neg_max[g][:, NB:2 * NB], in0=row_max[g][:, :], scalar=-1.0,
                                               in1=neg_max[g][:, 0:NB], op0=ALU.mult,
                                               op1=ALU.subtract).then_inc(max_split, 1)

            def copy_max_t(c, g):
                dve.wait_ge(max_turned, 2 * c + g + 1)
                nc.vector.tensor_copy(neg_max_t[g][0:2 * NB, :],
                                      turned_bf[g][0:2 * NB, 0:P]).then_inc(max_t_copied, 1)

            def combine(c, g, par):
                n = 2 * c + g + 1
                acc = attn_ps[g][:, 0:T * H * VW].rearrange("p (t h d) -> p t h d", t=T, h=H)
                dve.wait_ge(attn_ready, n)
                nc.vector.reciprocal(recip[g][:, :, :], acc[:, :, :, DH:VW].rearrange("p t h o -> p t (h o)")
                                     ).then_inc(recip_done, 1)
                dve.wait_ge(recip_done, n)
                nc.vector.scalar_tensor_tensor(
                    out=attn[g][:, :, :].rearrange("p t (h d) -> p (t h) d", h=H),
                    in0=acc[:, :, :, 0:DH].rearrange("p t h d -> p (t h) d"), scalar=0.0,
                    in1=recip[g][:, :, :].rearrange("p t h -> p (t h)").unsqueeze(2).to_broadcast([P, T * H, DH]),
                    op0=ALU.max, op1=ALU.mult).then_inc(attn_normed, 1)
                dve.wait_ge(attn_normed, n)
                nc.vector.tensor_tensor(
                    y[par][:, g * T:(g + 1) * T, :].rearrange("p t (b d) -> p t b d", b=2),
                    attn[g][:, :, :].rearrange("p t (b d) -> p t b d", b=2),
                    vr[par][:, :, g, 2:4, 0:DH], ALU.add).then_inc(y_added, 1)

            def moments_of(c, par, g):
                dve.wait_ge(y_added, 2 * c + g + 1)
                for n in range(g * T, (g + 1) * T):
                    last = nc.vector.bn_stats(stats[:, n, :], y[par][:, n, :])
                last.then_inc(stats_done, 1)

            def finish_moments(c, par):
                dve.wait_ge(stats_done, 2 * c + 2)
                dve.nop(nofuse=True)
                for n in range(GT):
                    last = nc.vector.bn_aggr(moments[par][:, n, :], stats[:, n, :])
                last.then_inc(moments_done, 1)

            def post(c, par, y_used=None):
                if y_used is not None:
                    dve.wait_ge(scaled_done, y_used)
                combine(c, 0, par)
                moments_of(c, par, 0)

            def post2(c, par):
                combine(c, 1, par)
                moments_of(c, par, 1)
                finish_moments(c, par)

            def step(c, par, kind):
                maxima(c, 0)
                maxima(c, 1)
                copy_max_t(c, 0)
                if kind == "first":
                    copy_max_t(c, 1)
                    return
                post(c - 1, 1 - par, None if kind == "early" else c - 2)
                copy_max_t(c, 1)
                post2(c - 1, 1 - par)

            step(0, 0, "first")
            step(1, 1, "early")
            step(2, 0, "early")
            with dve.Fori(1, n_chunks // 2 - 1) as pair:
                step(2 * pair + 1, 1, "middle")
                step(2 * pair + 2, 0, "middle")
            step(n_chunks - 1, 1, "middle")
            post(n_chunks - 1, 1, n_chunks - 2)
            post2(n_chunks - 1, 1)

        @block.tensor
        def _(pe):
            pe.wait_ge(const_loaded, 16 * (N_CONST_DMAS))
            pe.wait_ge(const_made, 2)

            def turn_x(c, par, xn, prev):
                pe.wait_ge(x_loaded[par], xn)
                if prev is not None:
                    pe.wait_ge(vr_copied, prev - 1)
                for t in range(T):
                    last = nc.tensor.transpose(front[par][:, t * P:(t + 1) * P],
                                               x_in[par][:, t, :, :].rearrange("p g e -> p (g e)"), ident[:, :])
                last.then_inc(xt_ready, 1)

            def project_q(c, par, prev):
                pe.wait_ge(xt_copied, c + 1)
                if prev is not None:
                    pe.wait_ge(vr_copied, prev)
                nc.tensor.matmul(front[1 - par][:, :], wq[:, :], xt[:, :], start=True, stop=True).then_inc(q_ready, 1)

            def project_k(c, par):
                nc.tensor.matmul(front[par][:, :], wk[:, :], xt[:, :], start=True, stop=True).then_inc(k_ready, 1)

            def project_vr(c, u, par):
                pe.wait_ge(q_copied if u == 0 else k_copied, c + 1)
                b = front[(par + 3 + u) % 2]
                nc.tensor.matmul(b[:, :], bias_rows[:, :], vr_bias[:, :], start=True, stop=False,
                                 skip_group_check=True)
                for i in range(2):
                    t = 2 * u + i
                    last = nc.tensor.matmul(b[:, i * 256:(i + 1) * 256], xt[:, t * P:(t + 1) * P],
                                            wvr[:, :, :].rearrange("p g e -> p (g e)"), start=False, stop=(i == 1),
                                            skip_group_check=True)
                last.then_inc(vr_ready, 1)

            def scores(c, g, first):
                r = slice(g * E, (g + 1) * E)
                if not first:
                    pe.wait_ge(exp_done, 2 * (c - 1) + g + 1)
                for n in range(NB):
                    last = nc.tensor.matmul(score[g][:, n * F:(n + 1) * F],
                                            q_t[r, n, :, :].rearrange("k h q -> k (h q)"),
                                            k_t[r, n * F:(n + 1) * F], start=(n == 0), stop=False,
                                            skip_group_check=True)
                last.then_inc(scores_ready, 1)

            def turn_max(c, g, first):
                pe.wait_ge(max_split, 2 * c + g + 1)
                if not first:
                    pe.wait_ge(probs_t_copied, 2 * (c - 1) + g + 1)
                nc.tensor.transpose(turned_bf[g][0:2 * NB, 0:P], neg_max[g][:, :], ident_bf[:, :]
                                    ).then_inc(max_turned, 1)

            def shift(c, g):
                pe.wait_ge(max_t_copied, 2 * c + g + 1)
                nc.tensor.matmul(score[g][:, :], neg_max_t[g][:, :], max_select[:, :], start=False, stop=True,
                                 skip_group_check=True).then_inc(shifted_ready, 1)

            def turn_probs(c, g):
                pe.wait_ge(exp_done, 2 * c + g + 1)
                for t in range(T):
                    last = nc.tensor.transpose(turned[g][:, t * P:(t + 1) * P], probs[g][:, t * P:(t + 1) * P],
                                               ident[:, :])
                last.then_inc(probs_turned, 1)

            def attend(c, g, par, early):
                pe.wait_ge(probs_t_copied, 2 * c + g + 1)
                pe.wait_ge(vr_copied, 2 * c + 2)
                if not early:
                    pe.wait_ge(attn_normed, 2 * (c - 1) + g + 1)
                pe.nop(nofuse=True)
                for t in range(T):
                    for h in range(H):
                        for b in range(2):
                            r = slice(b * F, (b + 1) * F)
                            col = (t * H + h) * VW
                            last = nc.tensor.matmul(
                                attn_ps[g][r, col:col + VW], probs_t[g][r, t * P + h * F:t * P + (h + 1) * F],
                                vr[par][r, t, g, h, :], start=True, stop=True)
                last.then_inc(attn_ready, 1)

            def step(c, par, kind):
                first, last = kind == "first", kind == "last"
                nxt = 1 - par
                pe.wait_ge(q_copied, c + 1)
                pe.wait_ge(k_copied, c + 1)
                for g in range(G):
                    scores(c, g, first)
                if not last:
                    turn_x(c + 1, nxt, 16 * (c + 1 - nxt) + 32, 2 * (c + 1))
                turn_max(c, 0, first)
                if not first:
                    attend(c - 1, 0, nxt, kind == "early")
                shift(c, 0)
                turn_max(c, 1, first)
                if not last:
                    project_q(c + 1, nxt, 2 * (c + 1))
                shift(c, 1)
                if not first:
                    attend(c - 1, 1, nxt, kind == "early")
                turn_probs(c, 0)
                if not last:
                    project_k(c + 1, nxt)
                turn_probs(c, 1)
                if not last:
                    project_vr(c + 1, 0, nxt)
                    project_vr(c + 1, 1, nxt)

            turn_x(0, 0, 32, None)
            project_q(0, 0, None)
            project_k(0, 0)
            project_vr(0, 0, 0)
            project_vr(0, 1, 0)
            step(0, 0, "first")
            step(1, 1, "early")
            step(2, 0, "middle")
            with pe.Fori(1, n_chunks // 2 - 1) as pair:
                step(2 * pair + 1, 1, "middle")
                step(2 * pair + 2, 0, "middle")
            step(n_chunks - 1, 1, "last")
            attend(n_chunks - 1, 0, 1, False)
            attend(n_chunks - 1, 1, 1, False)


_INS = ["r_input_emb", "L0_rec_QW", "L0_rec_Qb", "L0_rec_KW", "L0_rec_Kb", "L0_rec_VW", "L0_rec_Vb", "L0_rec_RW",
        "L0_rec_Rb", "L0_rec_gamma", "L0_rec_beta"]


def kernel(**inputs):
    import numpy as _np
    import concourse.bacc as _bacc
    from concourse import mybir as _mybir
    from concourse.bass_utils import run_bass_kernel_spmd as _run

    nc = _bacc.Bacc("TRN2", target_bir_lowering=False, num_devices=1)
    arrays, args = {}, []
    for name in _INS:
        a = _np.ascontiguousarray(inputs[name])
        arrays[f"in_{name}_dram"] = a
        args.append(nc.dram_tensor(f"in_{name}_dram", a.shape, _mybir.dt.from_np(a.dtype), kind="ExternalInput").ap())
    out = nc.dram_tensor("out_0_dram", arrays["in_r_input_emb_dram"].shape, _mybir.dt.float32, kind="ExternalOutput").ap()
    rec_attention(nc, *args, out)
    r = _run(nc, [arrays], core_ids=[0])
    return r.results[0]["out_0_dram"]
```

```python
from contextlib import ExitStack

import concourse.bass as bass
from concourse import mybir

ALU = mybir.AluOpType
ACT = mybir.ActivationFunctionType
AX_X = mybir.AxisListType.X
BF16 = mybir.dt.bfloat16
F32 = mybir.dt.float32

P = 128
F = 64
E = 64
H = 2
DH = E // H
G = 2
NB = 8
COLS = NB * F
CHUNK = G * COLS
T = COLS // P
U = 2
NU = NB // U
VR = 2 * E
VW = DH + 1
EPS = 1e-08
UNROLL = 4


def rec_attention(nc, x, qw, qb, kw, kb, vw, vb, rw, rb, gamma, beta, out):
    n_batch, _, _ = x.shape
    n_chunks = n_batch * F // CHUNK
    assert n_chunks * CHUNK == n_batch * F and n_chunks % UNROLL == 0 and n_chunks >= 2 * UNROLL
    scale = float(DH) ** -0.5

    x_view = x.rearrange("b f e -> (b f) e").rearrange("(c g t p) e -> c g p t e", g=G, t=T, p=P)
    out_view = out.rearrange("b f e -> (b f) e").rearrange("(c g n q) e -> c g q n e", g=G, n=NB, q=F)

    with ExitStack() as ctx:
        def sb(name, shape, dt=F32):
            return ctx.enter_context(nc.sbuf_tensor(name, shape, dt))

        def bank(name):
            return ctx.enter_context(nc.psum_tensor(name, [P, 512], F32))

        def sem(name):
            return ctx.enter_context(nc.semaphore(name))

        ident = sb("ident", [P, P])
        wq = sb("wq", [P, P])
        wk = sb("wk", [P, P])
        wvr = sb("wvr", [P, VR])
        head_mask = sb("head_mask", [P, H])
        q_bias = sb("q_bias", [P, 1])
        q_bias_masked = sb("q_bias_masked", [P, H])
        k_bias = sb("k_bias", [P, 1])
        vr_bias = sb("vr_bias", [P, VR])
        eps_all = sb("eps_all", [P, NB])
        minus_half = sb("minus_half", [P, NB])
        gamma_all = sb("gamma_all", [P, E])
        beta_all = sb("beta_all", [P, E])

        x_in = [sb(f"x_in{i}", [P, T, G, E]) for i in range(2)]
        xt = sb("xt", [P, COLS])
        xt_split = sb("xt_split", [P, NB, G, F])
        q_t = sb("q_t", [P, NB, H, F])
        k_t = sb("k_t", [P, NB, G, F])
        vr_raw = [sb(f"vr_raw{u}", [P, NU, VR]) for u in range(U)]
        vr = [sb(f"vr{i}", [P, NB, 4, VW]) for i in range(2)]
        row_max = [sb(f"row_max{u}", [P, NU * G]) for u in range(U)]
        shifted = [sb(f"shifted{u}", [P, NU * G, F]) for u in range(U)]
        probs = [sb(f"probs{u}", [P, NU, P]) for u in range(U)]
        probs_t = [sb(f"probs_t{u}", [P, NU, H, F]) for u in range(U)]
        recip = [sb(f"recip{u}", [P, NU, H]) for u in range(U)]
        attn = [sb(f"attn{u}", [P, NU, E]) for u in range(U)]
        y = [sb(f"y{i}", [P, NB, E]) for i in range(2)]
        stats = sb("stats", [P, NB, 6])
        moments = [sb(f"moments{i}", [P, NB, 2]) for i in range(2)]
        var_eps = sb("var_eps", [P, NB])
        rstd = sb("rstd", [P, NB])
        centred = sb("centred", [P, NB, E])
        normed = sb("normed", [P, NB, E])
        scaled = sb("scaled", [P, NB, E])
        y_out = [sb(f"y_out{i}", [P, NB, E]) for i in range(2)]

        front = [bank(f"front{i}") for i in range(2)]
        score = [bank(f"score{u}") for u in range(U)]
        turned = [bank(f"turned{u}") for u in range(U)]
        attn_ps = [bank(f"attn_ps{u}") for u in range(U)]

        const_zeroed = sem("const_zeroed")
        const_loaded = sem("const_loaded")
        const_made = sem("const_made")
        x_loaded = [sem(f"x_loaded{i}") for i in range(2)]
        xt_ready = sem("xt_ready")
        xt_copied = sem("xt_copied")
        xt_split_copied = sem("xt_split_copied")
        q_ready = sem("q_ready")
        q_copied = sem("q_copied")
        k_ready = sem("k_ready")
        k_copied = sem("k_copied")
        vr_ready = sem("vr_ready")
        vr_biased = sem("vr_biased")
        vr_copied = sem("vr_copied")
        scores_ready = sem("scores_ready")
        max_found = sem("max_found")
        shift_done = sem("shift_done")
        exp_done = sem("exp_done")
        probs_turned = sem("probs_turned")
        probs_t_copied = sem("probs_t_copied")
        attn_ready = sem("attn_ready")
        recip_done = sem("recip_done")
        attn_normed = sem("attn_normed")
        y_added = sem("y_added")
        stats_done = sem("stats_done")
        moments_done = sem("moments_done")
        var_eps_done = sem("var_eps_done")
        rstd_done = sem("rstd_done")
        centred_done = sem("centred_done")
        normed_done = sem("normed_done")
        scaled_done = sem("scaled_done")
        result_done = sem("result_done")
        stored = [sem(f"stored{i}") for i in range(2)]

        N_CONST_DMAS = 8 * G + 2
        block = ctx.enter_context(nc.Block())

        @block.sync
        def _(sp):
            sp.wait_ge(const_zeroed, 1)
            for g in range(G):
                r = slice(g * E, (g + 1) * E)
                for dst, src in (
                    (wq[r, r], qw), (wk[r, r], kw), (wvr[r, 0:E], vw), (wvr[r, E:VR], rw),
                    (q_bias[r, :], qb.rearrange("(e o) -> e o", o=1)),
                    (k_bias[r, :], kb.rearrange("(e o) -> e o", o=1)),
                    (vr_bias[r, 0:E], vb.partition_broadcast(E)),
                    (vr_bias[r, E:VR], rb.partition_broadcast(E)),
                ):
                    sp.dma_start(dst, src).then_inc(const_loaded, 16)
            sp.dma_start(gamma_all[:, :], gamma.partition_broadcast(P)).then_inc(const_loaded, 16)
            sp.dma_start(beta_all[:, :], beta.partition_broadcast(P)).then_inc(const_loaded, 16)

            def load(c, slot):
                for g in range(G):
                    sp.dma_start(x_in[slot][:, :, g, :], x_view[c, g]).then_inc(x_loaded[slot], 16)

            def store(c, slot):
                sp.wait_ge(result_done, c + 1)
                for g in range(G):
                    sp.dma_start(out_view[c, g], y_out[slot][g * F:(g + 1) * F, :, :]).then_inc(stored[slot], 16)

            load(0, 0)
            load(1, 1)
            sp.wait_ge(xt_ready, 1)
            load(2, 0)
            sp.wait_ge(xt_ready, 2)
            load(3, 1)
            with sp.Fori(0, n_chunks // 2 - 2) as pair:
                c = 2 * pair
                for k in range(2):
                    sp.wait_ge(xt_ready, c + k + 3)
                    load(c + k + 4, k)
                    store(c + k, k)
            for c in range(n_chunks - 4, n_chunks):
                store(c, c % 2)
            for k in range(2):
                sp.wait_ge(stored[k], 32 * (n_chunks // 2))

        @block.gpsimd
        def _(pool):
            for m in (wq, wk, ident, xt_split, q_t, k_t):
                last = nc.gpsimd.memset(m[:], 0.0)
            last.then_inc(const_zeroed, 1)
            pool.wait_ge(const_zeroed, 1)
            nc.gpsimd.affine_select(out=ident[:, :], in_=ident[:, :], compare_op=ALU.not_equal, fill=1.0, base=0,
                                    pattern=[[-1, P]], channel_multiplier=1).then_inc(const_zeroed, 1)
            pool.wait_ge(const_zeroed, 2)
            for q in range(P // DH):
                for h in range(H):
                    last = nc.gpsimd.memset(head_mask[q * DH:(q + 1) * DH, h:h + 1], 1.0 if q % H == h else 0.0)
            last.then_inc(const_zeroed, 1)
            pool.wait_ge(const_zeroed, 3)
            nc.gpsimd.memset(eps_all[:, :], EPS)
            nc.gpsimd.memset(minus_half[:, :], -0.5)
            for i in range(2):
                last = nc.gpsimd.memset(vr[i][:], 1.0)
            last.then_inc(const_made, 1)
            pool.wait_ge(const_loaded, 16 * N_CONST_DMAS)

            def finish(c, slot):
                whole = [P, NB, E]
                mean = moments[slot][:, :, 0:1].to_broadcast(whole)
                pool.wait_ge(moments_done, c + 1)
                pool.tensor_tensor(var_eps[:, :].unsqueeze(2), moments[slot][:, :, 1:2],
                                   eps_all[:, :].unsqueeze(2), ALU.add).then_inc(var_eps_done, 1)
                pool.wait_ge(var_eps_done, c + 1)
                pool.tensor_tensor(rstd[:, :], var_eps[:, :], minus_half[:, :], ALU.pow).then_inc(rstd_done, 1)
                pool.tensor_tensor(centred[:, :, :], y[slot][:, :, :], mean, ALU.subtract).then_inc(centred_done, 1)
                pool.wait_ge(centred_done, c + 1)
                pool.wait_ge(rstd_done, c + 1)
                pool.tensor_tensor(normed[:, :, :], centred[:, :, :],
                                   rstd[:, :].unsqueeze(2).to_broadcast(whole),
                                   ALU.mult).then_inc(normed_done, 1)
                pool.wait_ge(normed_done, c + 1)
                pool.tensor_tensor(scaled[:, :, :], normed[:, :, :],
                                   gamma_all[:, :].unsqueeze(1).to_broadcast(whole),
                                   ALU.mult).then_inc(scaled_done, 1)
                pool.wait_ge(scaled_done, c + 1)

            def add_beta(c, slot):
                pool.tensor_tensor(y_out[slot][:, :, :], scaled[:, :, :],
                                   beta_all[:, :].unsqueeze(1).to_broadcast([P, NB, E]),
                                   ALU.add).then_inc(result_done, 1)

            for c in range(2):
                finish(c, c)
                add_beta(c, c)
            with pool.Fori(1, n_chunks // 2) as pair:
                for k in range(2):
                    finish(2 * pair + k, k)
                    pool.wait_ge(stored[k], 32 * pair)
                    add_beta(2 * pair + k, k)

        @block.scalar
        def _(act):
            act.wait_ge(const_made, 2)

            def copy_xt(c, par):
                act.wait_ge(xt_ready, c + 1)
                nc.scalar.activation(xt[:, :], front[par][:, :], ACT.Copy).then_inc(xt_copied, 1)
                for g in range(G):
                    r = slice(g * E, (g + 1) * E)
                    last = nc.scalar.activation(xt_split[r, :, g, :],
                                                front[par][r, :].rearrange("k (n q) -> k n q", n=NB), ACT.Copy)
                last.then_inc(xt_split_copied, 1)

            def relu_q(c, par):
                act.wait_ge(q_ready, c + 1)
                for h in range(H):
                    last = nc.scalar.activation(
                        q_t[:, :, h, :], front[1 - par][:, :].rearrange("k (n q) -> k n q", n=NB), ACT.Relu,
                        bias=q_bias_masked[:, h:h + 1], scale=head_mask[:, h:h + 1])
                last.then_inc(q_copied, 1)

            def relu_k(c, par):
                act.wait_ge(k_ready, c + 1)
                for g in range(G):
                    r = slice(g * E, (g + 1) * E)
                    last = nc.scalar.activation(k_t[r, :, g, :],
                                                front[par][r, :].rearrange("k (n q) -> k n q", n=NB), ACT.Relu,
                                                bias=k_bias[r, 0:1])
                last.then_inc(k_copied, 1)

            def relu_vr(c, u, par, fresh):
                act.wait_ge(vr_biased, 2 * c + u + 1)
                if not fresh:
                    act.wait_ge(attn_ready, 2 * (c - 2) + u + 1)
                    act.wait_ge(y_added, 2 * (c - 2) + u + 1)
                nc.scalar.activation(
                    vr[par][:, u * NU:(u + 1) * NU, :, 0:DH],
                    vr_raw[u][:, :, :].rearrange("p n (b d) -> p n b d", b=4), ACT.Relu).then_inc(vr_copied, 1)

            def exps(c, u):
                act.wait_ge(shift_done, 2 * c + u + 1)
                nc.scalar.activation(probs[u][:, :, :].rearrange("p n (g k) -> p (n g) k", g=G), shifted[u][:, :, :],
                                     ACT.Exp, scale=scale).then_inc(exp_done, 1)

            def copy_probs_t(c, u):
                act.wait_ge(probs_turned, 2 * c + u + 1)
                nc.scalar.activation(probs_t[u][:, :, :, :].rearrange("p n h q -> p (n h q)"), turned[u][:, :],
                                     ACT.Copy).then_inc(probs_t_copied, 1)

            def step(c, par, first=False, last=False):
                nxt = 1 - par
                if not last:
                    copy_xt(c + 1, nxt)
                    relu_q(c + 1, nxt)
                exps(c, 0)
                exps(c, 1)
                if not last:
                    relu_k(c + 1, nxt)
                copy_probs_t(c, 0)
                if not last:
                    relu_vr(c + 1, 0, nxt, first)
                copy_probs_t(c, 1)
                if not last:
                    relu_vr(c + 1, 1, nxt, first)

            copy_xt(0, 0)
            relu_q(0, 0)
            relu_k(0, 0)
            relu_vr(0, 0, 0, True)
            relu_vr(0, 1, 0, True)
            step(0, 0, first=True)
            step(1, 1)
            step(2, 0)
            with act.Fori(0, n_chunks // UNROLL - 1) as i:
                for k in range(3, 3 + UNROLL):
                    step(UNROLL * i + k, k % 2)
            step(n_chunks - 1, 1, last=True)

        @block.vector
        def _(dve):
            dve.wait_ge(const_loaded, 16 * N_CONST_DMAS)
            dve.wait_ge(const_made, 1)
            nc.vector.tensor_scalar(q_bias_masked[:, :], head_mask[:, :], q_bias[:, 0:1], None,
                                    ALU.mult).then_inc(const_made, 1)

            def shift(c, u):
                n = 2 * c + u + 1
                rows = score[u][:, :].rearrange("p (n k) -> p n k", n=NU * G)
                dve.wait_ge(scores_ready, n)
                nc.vector.tensor_reduce(row_max[u][:, :], rows, AX_X, ALU.max).then_inc(max_found, 1)
                dve.wait_ge(max_found, n)
                nc.vector.tensor_tensor(shifted[u][:, :, :], rows,
                                        row_max[u][:, :].unsqueeze(2).to_broadcast([P, NU * G, F]),
                                        ALU.subtract).then_inc(shift_done, 1)

            def bias_vr(c, u, par):
                dve.wait_ge(vr_ready, 2 * c + u + 1)
                nc.vector.tensor_tensor(
                    vr_raw[u][:, :, :], front[(1 - par + u) % 2][:, :].rearrange("p (n e) -> p n e", n=NU),
                    vr_bias[:, :].unsqueeze(1).to_broadcast([P, NU, VR]), ALU.add).then_inc(vr_biased, 1)

            def combine(c, u, par):
                n = 2 * c + u + 1
                acc = attn_ps[u][:, 0:NU * H * VW].rearrange("p (n d) -> p n d", n=NU * H)
                dve.wait_ge(attn_ready, n)
                nc.vector.reciprocal(recip[u][:, :, :].rearrange("p n h -> p (n h)").unsqueeze(2),
                                     acc[:, :, DH:VW]).then_inc(recip_done, 1)
                dve.wait_ge(recip_done, n)
                nc.vector.scalar_tensor_tensor(
                    out=attn[u][:, :, :].rearrange("p n (h d) -> p (n h) d", h=H), in0=acc[:, :, 0:DH], scalar=0.0,
                    in1=recip[u][:, :, :].rearrange("p n h -> p (n h)").unsqueeze(2).to_broadcast([P, NU * H, DH]),
                    op0=ALU.max, op1=ALU.mult).then_inc(attn_normed, 1)
                dve.wait_ge(attn_normed, n)
                nc.vector.tensor_tensor(
                    y[par][:, u * NU:(u + 1) * NU, :].rearrange("p n (b d) -> p n b d", b=2),
                    attn[u][:, :, :].rearrange("p n (b d) -> p n b d", b=2),
                    vr[par][:, u * NU:(u + 1) * NU, 2:4, 0:DH], ALU.add).then_inc(y_added, 1)

            def moments_of(c, u, par):
                dve.wait_ge(y_added, 2 * c + u + 1)
                for n in range(u * NU, (u + 1) * NU):
                    last = nc.vector.bn_stats(stats[:, n, :], y[par][:, n, :])
                last.then_inc(stats_done, 1)

            def finish_moments(c, par):
                dve.wait_ge(stats_done, 2 * c + 2)
                dve.nop(nofuse=True)
                for n in range(NB):
                    last = nc.vector.bn_aggr(moments[par][:, n, :], stats[:, n, :])
                last.then_inc(moments_done, 1)

            def step(c, par, kind):
                shift(c, 0)
                shift(c, 1)
                if kind != "first":
                    if kind == "middle":
                        dve.wait_ge(centred_done, c - 2)
                    combine(c - 1, 0, 1 - par)
                    moments_of(c - 1, 0, 1 - par)
                if kind != "last":
                    bias_vr(c + 1, 0, 1 - par)
                if kind != "first":
                    combine(c - 1, 1, 1 - par)
                if kind != "last":
                    bias_vr(c + 1, 1, 1 - par)
                if kind != "first":
                    moments_of(c - 1, 1, 1 - par)
                    finish_moments(c - 1, 1 - par)

            for u in range(U):
                bias_vr(0, u, 0)
            step(0, 0, "first")
            step(1, 1, "early")
            step(2, 0, "early")
            with dve.Fori(0, n_chunks // UNROLL - 1) as i:
                for k in range(3, 3 + UNROLL):
                    step(UNROLL * i + k, k % 2, "middle")
            dve.wait_ge(centred_done, n_chunks - 3)
            step(n_chunks - 1, 1, "last")
            dve.wait_ge(centred_done, n_chunks - 2)
            for u in range(U):
                combine(n_chunks - 1, u, 1)
                moments_of(n_chunks - 1, u, 1)
            finish_moments(n_chunks - 1, 1)

        @block.tensor
        def _(pe):
            pe.wait_ge(const_loaded, 16 * N_CONST_DMAS)
            pe.wait_ge(const_made, 2)

            def turn_x(c, par, loads, fresh):
                pe.wait_ge(x_loaded[par], loads)
                if not fresh:
                    pe.wait_ge(vr_biased, 2 * c - 1)
                for t in range(T):
                    last = nc.tensor.transpose(front[par][:, t * P:(t + 1) * P],
                                               x_in[par][:, t, :, :].rearrange("p g e -> p (g e)"), ident[:, :])
                last.then_inc(xt_ready, 1)

            def project_q(c, par, fresh):
                pe.wait_ge(xt_copied, c + 1)
                if not fresh:
                    pe.wait_ge(vr_biased, 2 * c)
                nc.tensor.matmul(front[1 - par][:, :], wq[:, :], xt[:, :], start=True, stop=True).then_inc(q_ready, 1)

            def project_k(c, par):
                pe.wait_ge(xt_split_copied, c + 1)
                nc.tensor.matmul(front[par][:, :], wk[:, :], xt[:, :], start=True, stop=True).then_inc(k_ready, 1)

            def project_vr(c, u, par):
                pe.wait_ge(q_copied if u == 0 else k_copied, c + 1)
                b = front[(1 - par + u) % 2]
                for n in range(NU):
                    last = nc.tensor.matmul(b[:, n * VR:(n + 1) * VR],
                                            xt_split[:, u * NU + n, :, :].rearrange("k g q -> k (g q)"),
                                            wvr[:, :], start=True, stop=True)
                last.then_inc(vr_ready, 1)

            def scores(c, u, first):
                if not first:
                    pe.wait_ge(shift_done, 2 * (c - 1) + u + 1)
                for n in range(NU):
                    last = nc.tensor.matmul(score[u][:, n * P:(n + 1) * P],
                                            q_t[:, u * NU + n, :, :].rearrange("k h q -> k (h q)"),
                                            k_t[:, u * NU + n, :, :].rearrange("k g q -> k (g q)"),
                                            start=True, stop=True)
                last.then_inc(scores_ready, 1)

            def turn_probs(c, u, first):
                pe.wait_ge(exp_done, 2 * c + u + 1)
                if not first:
                    pe.wait_ge(probs_t_copied, 2 * (c - 1) + u + 1)
                for n in range(NU):
                    last = nc.tensor.transpose(turned[u][:, n * P:(n + 1) * P], probs[u][:, n, :], ident[:, :])
                last.then_inc(probs_turned, 1)

            def attend(c, u, par, early):
                pe.wait_ge(probs_t_copied, 2 * c + u + 1)
                pe.wait_ge(vr_copied, 2 * c + u + 1)
                if not early:
                    pe.wait_ge(attn_normed, 2 * (c - 1) + u + 1)
                pe.nop(nofuse=True)
                for n in range(NU):
                    for h in range(H):
                        for g in range(G):
                            r = slice(g * F, (g + 1) * F)
                            col = (n * H + h) * VW
                            last = nc.tensor.matmul(attn_ps[u][r, col:col + VW], probs_t[u][r, n, h, :],
                                                    vr[par][r, u * NU + n, h, :], start=True, stop=True)
                last.then_inc(attn_ready, 1)

            def step(c, par, kind):
                first, last, early = kind == "first", kind == "last", kind == "early"
                nxt = 1 - par
                pe.wait_ge(q_copied, c + 1)
                pe.wait_ge(k_copied, c + 1)
                scores(c, 0, first)
                if not last:
                    turn_x(c + 1, nxt, 16 * (c + 1 - nxt) + 32, False)
                scores(c, 1, first)
                if not last:
                    project_q(c + 1, nxt, False)
                if not first:
                    attend(c - 1, 0, nxt, early)
                if not last:
                    project_k(c + 1, nxt)
                turn_probs(c, 0, first)
                if not last:
                    project_vr(c + 1, 0, nxt)
                if not first:
                    attend(c - 1, 1, nxt, early)
                turn_probs(c, 1, first)
                if not last:
                    project_vr(c + 1, 1, nxt)

            turn_x(0, 0, 32, True)
            project_q(0, 0, True)
            project_k(0, 0)
            project_vr(0, 0, 0)
            project_vr(0, 1, 0)
            step(0, 0, "first")
            step(1, 1, "early")
            step(2, 0, "middle")
            with pe.Fori(0, n_chunks // UNROLL - 1) as i:
                for k in range(3, 3 + UNROLL):
                    step(UNROLL * i + k, k % 2, "middle")
            step(n_chunks - 1, 1, "last")
            for u in range(U):
                attend(n_chunks - 1, u, 1, False)


_INS = ["r_input_emb", "L0_rec_QW", "L0_rec_Qb", "L0_rec_KW", "L0_rec_Kb", "L0_rec_VW", "L0_rec_Vb", "L0_rec_RW",
        "L0_rec_Rb", "L0_rec_gamma", "L0_rec_beta"]


def kernel(**inputs):
    import numpy as _np
    import concourse.bacc as _bacc
    from concourse import mybir as _mybir
    from concourse.bass_utils import run_bass_kernel_spmd as _run

    nc = _bacc.Bacc("TRN2", target_bir_lowering=False, num_devices=1)
    arrays, args = {}, []
    for name in _INS:
        a = _np.ascontiguousarray(inputs[name])
        arrays[f"in_{name}_dram"] = a
        args.append(nc.dram_tensor(f"in_{name}_dram", a.shape, _mybir.dt.from_np(a.dtype), kind="ExternalInput").ap())
    out = nc.dram_tensor("out_0_dram", arrays["in_r_input_emb_dram"].shape, _mybir.dt.float32, kind="ExternalOutput").ap()
    rec_attention(nc, *args, out)
    r = _run(nc, [arrays], core_ids=[0])
    return r.results[0]["out_0_dram"]
```

```python
from contextlib import ExitStack

from concourse import mybir

ALU = mybir.AluOpType
ACT = mybir.ActivationFunctionType
AX_X = mybir.AxisListType.X
F32 = mybir.dt.float32
F32R = mybir.dt.float32r

P = 128
F = 64
E = 64
H = 2
DH = E // H
G = 2
NB = 8
CHUNK = NB * P
PARTS = 2
U = 2
NU = NB // U
VR = 2 * E
VW = DH + 1
EPS = 1e-08
UNROLL = 4


def rec_attention(nc, x, qw, qb, kw, kb, vw, vb, rw, rb, gamma, beta, out):
    n_batch, _, _ = x.shape
    n_chunks = n_batch * F // CHUNK
    assert n_chunks * CHUNK == n_batch * F and n_chunks % UNROLL == 0 and n_chunks > 2 * UNROLL
    scale = float(DH) ** -0.5

    x_view = x.rearrange("b f e -> (b f) e").rearrange("(c n p) e -> c p n e", n=NB, p=P)
    out_view = out.rearrange("b f e -> (b f) e").rearrange("(c n p) e -> c p n e", n=NB, p=P)

    with ExitStack() as ctx:
        def sb(name, shape, dt=F32):
            return ctx.enter_context(nc.sbuf_tensor(name, shape, dt))

        def bank(name):
            return ctx.enter_context(nc.psum_tensor(name, [P, 512], F32))

        def sem(name):
            return ctx.enter_context(nc.semaphore(name))

        ident = sb("ident", [P, P])
        ident_r = sb("ident_r", [P, P], F32R)
        wqk = sb("wqk", [P, G, P])
        wqk_high = sb("wqk_high", [P, G, P], F32R)
        wqk_low = sb("wqk_low", [P, G, P], F32R)
        qk_bias = sb("qk_bias", [P, G])
        wvr = sb("wvr", [P, VR])
        vr_bias = sb("vr_bias", [P, VR])
        eps_all = sb("eps_all", [P, NB])
        minus_half = sb("minus_half", [P, NB])
        gamma_all = sb("gamma_all", [P, E])
        beta_all = sb("beta_all", [P, E])

        x_in = [sb(f"x_in{i}", [P, NB, E]) for i in range(2)]
        x_parts = [sb(f"x_parts{i}", [P, NB, PARTS, E], F32R) for i in range(2)]
        xt = sb("xt", [P, NB, P], F32R)
        q_t = [sb(f"q_t{i}", [P, NB, G, F]) for i in range(2)]
        k_t = [sb(f"k_t{i}", [P, NB, H, F]) for i in range(2)]
        vr_raw = [sb(f"vr_raw{i}", [P, NB, VR]) for i in range(UNROLL)]
        v = [sb(f"v{i}", [P, NB, G, H, VW]) for i in range(2)]
        row_max = [sb(f"row_max{u}", [P, NU * H]) for u in range(U)]
        shifted = [sb(f"shifted{u}", [P, NU * H, F]) for u in range(U)]
        probs = [sb(f"probs{u}", [P, NU, P]) for u in range(U)]
        probs_t = [sb(f"probs_t{i}", [P, NB, G, F]) for i in range(2)]
        recip = sb("recip", [P, NB * H])
        attn = sb("attn", [P, NB, E])
        y = [sb(f"y{i}", [P, NB, E]) for i in range(2)]
        stats = sb("stats", [P, NB, 6])
        moments = [sb(f"moments{i}", [P, NB, 2]) for i in range(2)]
        var_eps = [sb(f"var_eps{i}", [P, NB]) for i in range(2)]
        rstd = [sb(f"rstd{i}", [P, NB]) for i in range(2)]
        centred = sb("centred", [P, NB, E])
        normed = sb("normed", [P, NB, E])
        scaled = sb("scaled", [P, NB, E])
        y_out = [sb(f"y_out{i}", [P, NB, E]) for i in range(2)]

        front = ctx.enter_context(nc.psum_tensor("front", [P, 3, 512], F32))
        QK_BANK = 2
        score = [bank(f"score{u}") for u in range(U)]
        turned = bank("turned")
        attn_ps = ctx.enter_context(nc.psum_tensor("attn_ps", [P, U, 512], F32))

        const_zeroed = sem("const_zeroed")
        const_loaded = sem("const_loaded")
        const_made = sem("const_made")
        x_loaded = [sem(f"x_loaded{i}") for i in range(2)]
        x_high_made = sem("x_high_made")
        x_low_made = sem("x_low_made")
        xt_ready = sem("xt_ready")
        xt_copied = sem("xt_copied")
        qk_ready = sem("qk_ready")
        qk_copied = sem("qk_copied")
        vr_ready = sem("vr_ready")
        vr_biased = sem("vr_biased")
        v_copied_act = sem("v_copied_act")
        v_copied_dve = sem("v_copied_dve")
        scores_ready = sem("scores_ready")
        max_found = sem("max_found")
        shift_done = sem("shift_done")
        exp_done = sem("exp_done")
        probs_turned = sem("probs_turned")
        probs_t_copied = sem("probs_t_copied")
        attn_ready = sem("attn_ready")
        recip_done = sem("recip_done")
        attn_normed = sem("attn_normed")
        y_added = sem("y_added")
        stats_done = sem("stats_done")
        moments_done = sem("moments_done")
        var_eps_done = sem("var_eps_done")
        rstd_done = sem("rstd_done")
        y_free = sem("y_free")
        normed_done = sem("normed_done")
        scaled_done = sem("scaled_done")
        result_done = sem("result_done")
        stored = [sem(f"stored{i}") for i in range(2)]

        ACT_V, DVE_V = ((0, 0), (0, 1), (1, 0)), (1, 1)

        def v_of(par, g, h):
            return v[par][h * F:(h + 1) * F, :, g, h, 0:DH]

        def raw_v_of(slot, g, h):
            return vr_raw[slot][g * F:(g + 1) * F, :, h * DH:(h + 1) * DH]

        N_CONST_DMAS = 10 * PARTS + 2
        block = ctx.enter_context(nc.Block())

        @block.sync
        def _(sp):
            for part in range(PARTS):
                r = slice(part * E, (part + 1) * E)
                q_column, k_column = part, 1 - part
                for dst, src in (
                    (wqk[r, 0, 0:E], qw), (wqk[r, 0, E:P], kw), (wqk[r, 1, 0:E], kw), (wqk[r, 1, E:P], qw),
                    (wvr[r, 0:E], vw), (wvr[r, E:VR], rw),
                    (qk_bias[r, q_column:q_column + 1], qb.rearrange("(e o) -> e o", o=1)),
                    (qk_bias[r, k_column:k_column + 1], kb.rearrange("(e o) -> e o", o=1)),
                    (vr_bias[r, 0:E], vb.partition_broadcast(E)),
                    (vr_bias[r, E:VR], rb.partition_broadcast(E)),
                ):
                    sp.dma_start(dst, src).then_inc(const_loaded, 16)
            sp.dma_start(gamma_all[:, :], gamma.partition_broadcast(P)).then_inc(const_loaded, 16)
            sp.dma_start(beta_all[:, :], beta.partition_broadcast(P)).then_inc(const_loaded, 16)

            def load(c, slot):
                sp.dma_start(x_in[slot][:, :, :], x_view[c]).then_inc(x_loaded[slot], 16)

            def store(c, slot):
                sp.wait_ge(result_done, c + 1)
                sp.dma_start(out_view[c], y_out[slot][:, :, :]).then_inc(stored[slot], 16)

            load(0, 0)
            load(1, 1)
            for c in range(2, 7):
                sp.wait_ge(x_low_made, c - 1)
                load(c, c % 2)
            with sp.Fori(0, n_chunks // 2 - 4) as pair:
                for k in range(2):
                    sp.wait_ge(x_low_made, 2 * pair + k + 6)
                    load(2 * pair + k + 7, 1 - k)
                    store(2 * pair + k, k)
            sp.wait_ge(x_low_made, n_chunks - 2)
            load(n_chunks - 1, 1)
            for c in range(n_chunks - 8, n_chunks):
                store(c, c % 2)
            for k in range(2):
                sp.wait_ge(stored[k], 16 * (n_chunks // 2))

        @block.gpsimd
        def _(pool):
            for m in (ident, *q_t, *k_t, *v):
                last = nc.gpsimd.memset(m[:], 0.0)
            last.then_inc(const_zeroed, 1)
            pool.wait_ge(const_zeroed, 1)
            nc.gpsimd.affine_select(out=ident[:, :], in_=ident[:, :], compare_op=ALU.not_equal, fill=1.0, base=0,
                                    pattern=[[-1, P]], channel_multiplier=1).then_inc(const_zeroed, 1)
            nc.gpsimd.memset(eps_all[:, :], EPS)
            nc.gpsimd.memset(minus_half[:, :], -0.5).then_inc(const_zeroed, 1)
            pool.wait_ge(const_zeroed, 3)
            for h in range(H):
                for i in range(2):
                    last = nc.gpsimd.memset(v[i][h * F:(h + 1) * F, :, :, h, DH:VW], 1.0)
                last.then_inc(const_zeroed, 1)
                pool.wait_ge(const_zeroed, 4 + h)
            nc.gpsimd.nop(nofuse=True).then_inc(const_made, 1)
            pool.wait_ge(const_loaded, 16 * N_CONST_DMAS)

            def find_rstd(c, slot):
                pool.wait_ge(var_eps_done, c + 1)
                pool.tensor_tensor(rstd[slot][:, :], var_eps[slot][:, :], minus_half[:, :],
                                   ALU.pow).then_inc(rstd_done, 1)

            def centre(c, slot):
                pool.wait_ge(rstd_done, c + 1)
                pool.tensor_tensor(centred[:, :, :], y[slot][:, :, :],
                                   moments[slot][:, :, 0:1].to_broadcast([P, NB, E]),
                                   ALU.subtract).then_inc(y_free, 1)

            def scale_rows(c, slot):
                pool.wait_ge(y_free, c + 1)
                pool.tensor_tensor(normed[:, :, :], centred[:, :, :],
                                   rstd[slot][:, :].unsqueeze(2).to_broadcast([P, NB, E]),
                                   ALU.mult).then_inc(normed_done, 1)
                pool.wait_ge(normed_done, c + 1)
                pool.tensor_tensor(scaled[:, :, :], normed[:, :, :],
                                   gamma_all[:, :].unsqueeze(1).to_broadcast([P, NB, E]),
                                   ALU.mult).then_inc(scaled_done, 1)

            def add_beta(c, slot):
                pool.wait_ge(scaled_done, c + 1)
                pool.tensor_tensor(y_out[slot][:, :, :], scaled[:, :, :],
                                   beta_all[:, :].unsqueeze(1).to_broadcast([P, NB, E]),
                                   ALU.add).then_inc(result_done, 1)

            def split_low(c, slot):
                pool.wait_ge(x_high_made, c + 1)
                pool.tensor_tensor(x_parts[slot][:, :, 1, :], x_in[slot][:, :, :],
                                   x_parts[slot][:, :, 0, :].bitcast(F32), ALU.subtract).then_inc(x_low_made, 1)

            for c in range(5):
                split_low(c, c % 2)
            find_rstd(0, 0)
            for c in range(2):
                centre(c, c)
                split_low(c + 5, 1 - c)
                scale_rows(c, c)
                find_rstd(c + 1, 1 - c)
                add_beta(c, c)
            with pool.Fori(1, n_chunks // 2 - 3) as pair:
                for k in range(2):
                    centre(2 * pair + k, k)
                    split_low(2 * pair + k + 5, 1 - k)
                    scale_rows(2 * pair + k, k)
                    find_rstd(2 * pair + k + 1, 1 - k)
                    pool.wait_ge(stored[k], 16 * pair)
                    add_beta(2 * pair + k, k)
            for c in range(n_chunks - 6, n_chunks):
                centre(c, c % 2)
                if c + 5 < n_chunks:
                    split_low(c + 5, (c + 5) % 2)
                scale_rows(c, c % 2)
                if c + 1 < n_chunks:
                    find_rstd(c + 1, (c + 1) % 2)
                pool.wait_ge(stored[c % 2], 16 * (c // 2))
                add_beta(c, c % 2)

        @block.scalar
        def _(act):
            act.wait_ge(const_made, 1)
            act.wait_ge(const_loaded, 16 * N_CONST_DMAS)

            def copy_xt(c):
                act.wait_ge(xt_ready, 2 * c + 2)
                nc.scalar.activation(xt[:, :, :].rearrange("k (u n) p -> k u (n p)", u=U),
                                     front[:, 0:U, :].bitcast(F32R),
                                     ACT.Copy).then_inc(xt_copied, 1)

            def relu_q(c, g, par):
                act.wait_ge(qk_ready, 2 * c + g + 1)
                r = slice(g * E, (g + 1) * E)
                nc.scalar.activation(q_t[par][r, :, g, :], front[r, QK_BANK, :].rearrange("k (n q) -> k n q", n=NB),
                                     ACT.Relu, bias=qk_bias[r, g:g + 1])

            def relu_k(c, g, par):
                for h in range(H):
                    src = slice((1 - g) * E + h * DH, (1 - g) * E + (h + 1) * DH)
                    dst = slice(g * E + h * DH, g * E + (h + 1) * DH)
                    last = nc.scalar.activation(k_t[par][dst, :, h, :],
                                                front[src, QK_BANK, :].rearrange("k (n q) -> k n q", n=NB),
                                                ACT.Relu, bias=qk_bias[src, g:g + 1])
                last.then_inc(qk_copied, 1)

            def relu_v(c, par, slot, fresh):
                act.wait_ge(vr_biased, 2 * c + 2)
                if not fresh:
                    act.wait_ge(attn_ready, c - 1)
                for g, h in ACT_V:
                    last = nc.scalar.activation(v_of(par, g, h), raw_v_of(slot, g, h), ACT.Relu)
                last.then_inc(v_copied_act, 1)

            def exps(c, u):
                act.wait_ge(shift_done, 2 * c + u + 1)
                nc.scalar.activation(probs[u][:, :, :].rearrange("p n (h k) -> p (n h) k", h=H), shifted[u][:, :, :],
                                     ACT.Exp, scale=scale).then_inc(exp_done, 1)

            def copy_probs_t(c, u, par):
                act.wait_ge(probs_turned, 2 * c + u + 1)
                nc.scalar.activation(probs_t[par][:, u * NU:(u + 1) * NU, :, :].rearrange("p n g q -> p (n g q)"),
                                     turned[:, :], ACT.Copy).then_inc(probs_t_copied, 1)

            def step(c, par, slot, kind):
                first, last, early = kind == "first", kind == "last", kind in ("first", "second")
                if not last:
                    copy_xt(c + 1)
                if not first:
                    copy_probs_t(c - 1, 1, 1 - par)
                relu_v(c, par, slot, early)
                if not last:
                    relu_q(c + 1, 0, 1 - par)
                    relu_k(c + 1, 0, 1 - par)
                exps(c, 0)
                exps(c, 1)
                if not last:
                    relu_q(c + 1, 1, 1 - par)
                copy_probs_t(c, 0, par)
                if not last:
                    relu_k(c + 1, 1, 1 - par)

            copy_xt(0)
            for g in range(G):
                relu_q(0, g, 0)
                relu_k(0, g, 0)
            step(0, 0, 0, "first")
            step(1, 1, 1, "second")
            with act.Fori(0, n_chunks // UNROLL - 1) as i:
                for k in range(2, 2 + UNROLL):
                    step(UNROLL * i + k, k % 2, k % UNROLL, "middle")
            step(n_chunks - 2, 0, UNROLL - 2, "middle")
            step(n_chunks - 1, 1, UNROLL - 1, "last")
            copy_probs_t(n_chunks - 1, 1, 1)

        @block.vector
        def _(dve):
            dve.wait_ge(const_loaded, 16 * N_CONST_DMAS)
            dve.wait_ge(const_made, 1)
            nc.vector.tensor_copy(ident_r[:, :], ident[:, :])
            nc.vector.tensor_copy(wqk_high[:, :, :], wqk[:, :, :]).then_inc(const_made, 1)
            dve.wait_ge(const_made, 2)
            nc.vector.tensor_tensor(wqk_low[:, :, :], wqk[:, :, :], wqk_high[:, :, :].bitcast(F32),
                                    ALU.subtract).then_inc(const_made, 1)

            def split_high(c, slot, loads, fresh):
                dve.wait_ge(x_loaded[slot], loads)
                if not fresh:
                    dve.wait_ge(xt_ready, 2 * (c - 1))
                nc.vector.tensor_copy(x_parts[slot][:, :, 0, :], x_in[slot][:, :, :]).then_inc(x_high_made, 1)

            def scores_of(u):
                return score[u][:, :].rearrange("p (n k) -> p n k", n=NU * H)

            def find_max(c, u):
                dve.wait_ge(scores_ready, 2 * c + u + 1)
                nc.vector.tensor_reduce(row_max[u][:, :], scores_of(u), AX_X, ALU.max).then_inc(max_found, 1)

            def shift(c, u):
                dve.wait_ge(max_found, 2 * c + u + 1)
                nc.vector.tensor_tensor(shifted[u][:, :, :], scores_of(u),
                                        row_max[u][:, :].unsqueeze(2).to_broadcast([P, NU * H, F]),
                                        ALU.subtract).then_inc(shift_done, 1)

            def bias_vr(c, u, slot):
                dve.wait_ge(vr_ready, 2 * c + u + 1)
                nc.vector.tensor_tensor(
                    vr_raw[slot][:, u * NU:(u + 1) * NU, :], front[:, u, :].rearrange("p (n e) -> p n e", n=NU),
                    vr_bias[:, :].unsqueeze(1).to_broadcast([P, NU, VR]), ALU.add).then_inc(vr_biased, 1)

            acc = attn_ps[:, :, 0:NU * H * VW].rearrange("p u (n d) -> p u n d", n=NU * H)
            sums = recip[:, :].rearrange("p (u n) -> p u n", u=U).unsqueeze(3)

            def invert_sums(c):
                dve.wait_ge(attn_ready, c + 1)
                nc.vector.reciprocal(sums, acc[:, :, :, DH:VW]).then_inc(recip_done, 1)

            def divide(c):
                dve.wait_ge(recip_done, c + 1)
                nc.vector.tensor_tensor(
                    attn[:, :, :].rearrange("p (u n) (h d) -> p u (n h) d", u=U, h=H), acc[:, :, :, 0:DH],
                    sums.to_broadcast([P, U, NU * H, DH]), ALU.mult).then_inc(attn_normed, 1)

            def add_residual(c, par, slot, fresh):
                if not fresh:
                    dve.wait_ge(y_free, c - 1)
                dve.wait_ge(attn_normed, c + 1)
                nc.vector.scalar_tensor_tensor(
                    out=y[par][:, :, :], in0=vr_raw[slot][:, :, E:VR], scalar=0.0,
                    in1=attn[:, :, :], op0=ALU.max, op1=ALU.add).then_inc(y_added, 1)

            def block_stats(c, par, start, stop):
                dve.wait_ge(y_added, c + 1)
                for n in range(start, stop):
                    last = nc.vector.bn_stats(stats[:, n, :], y[par][:, n, :])
                if stop == NB:
                    last.then_inc(stats_done, 1)

            def find_moments(c, par):
                dve.wait_ge(stats_done, c + 1)
                dve.nop(nofuse=True)
                for n in range(NB):
                    last = nc.vector.bn_aggr(moments[par][:, n, :], stats[:, n, :])
                last.then_inc(moments_done, 1)

            def add_eps(c, par):
                dve.wait_ge(moments_done, c + 1)
                nc.vector.tensor_tensor(var_eps[par][:, :].unsqueeze(2), moments[par][:, :, 1:2],
                                        eps_all[:, :].unsqueeze(2), ALU.add).then_inc(var_eps_done, 1)

            def relu_v(c, par, slot):
                dve.wait_ge(vr_biased, 2 * c + 2)
                nc.vector.tensor_scalar(v_of(par, *DVE_V), raw_v_of(slot, *DVE_V), 0.0, None,
                                        ALU.max).then_inc(v_copied_dve, 1)

            def step(c, par, slot, done, before_end=3):
                if done >= 2:
                    invert_sums(c - 2)
                if done >= 3:
                    find_moments(c - 3, 1 - par)
                if done >= 2:
                    divide(c - 2)
                if done >= 3:
                    add_eps(c - 3, 1 - par)
                relu_v(c, par, slot)
                if done >= 2:
                    add_residual(c - 2, par, (slot - 2) % UNROLL, done < 4)
                find_max(c, 0)
                if done >= 2:
                    block_stats(c - 2, par, 0, 1)
                shift(c, 0)
                find_max(c, 1)
                if done >= 2:
                    block_stats(c - 2, par, 1, 2)
                shift(c, 1)
                if before_end >= 1:
                    for u in range(U):
                        bias_vr(c + 1, u, (slot + 1) % UNROLL)
                if before_end >= 3:
                    split_high(c + 3, 1 - par, 8 * (c + par) + 32, False)
                if done >= 2:
                    block_stats(c - 2, par, 2, NB)

            for c in range(2):
                split_high(c, c, 16, True)
            for u in range(U):
                bias_vr(0, u, 0)
            split_high(2, 0, 32, False)
            PEELED = UNROLL + 1
            for c in range(PEELED):
                step(c, c % 2, c % UNROLL, done=min(c, 4))
            with dve.Fori(0, n_chunks // UNROLL - 2) as i:
                for k in range(PEELED, PEELED + UNROLL):
                    step(UNROLL * i + k, k % 2, k % UNROLL, done=4)
            for before_end in (2, 1, 0):
                c = n_chunks - 1 - before_end
                step(c, c % 2, c % UNROLL, done=4, before_end=before_end)
            find_moments(n_chunks - 3, 1)
            add_eps(n_chunks - 3, 1)
            for c in range(n_chunks - 2, n_chunks):
                invert_sums(c)
                divide(c)
                add_residual(c, c % 2, c % UNROLL, False)
                block_stats(c, c % 2, 0, NB)
                find_moments(c, c % 2)
                add_eps(c, c % 2)

        @block.tensor
        def _(pe):
            pe.wait_ge(const_loaded, 16 * N_CONST_DMAS)
            pe.wait_ge(const_made, 3)

            def turn_x(c, par, fresh):
                pe.wait_ge(x_low_made, c + 1)
                for u in range(U):
                    if not fresh:
                        pe.wait_ge(vr_biased, 2 * (c - 1) + u + 1)
                    for n in range(NU):
                        last = nc.tensor.transpose(front[:, u, n * P:(n + 1) * P].bitcast(F32R),
                                                   x_parts[par][:, u * NU + n, :, :].rearrange("p a e -> p (a e)"),
                                                   ident_r[:, :])
                    last.then_inc(xt_ready, 1)

            def project_qk(c, g, fresh):
                pe.wait_ge(xt_copied, c + 1)
                if not fresh:
                    pe.wait_ge(qk_copied, 2 * c + g)
                tokens = xt[:, :, g * F:(g + 1) * F]
                nc.tensor.matmul(front[:, QK_BANK, :], wqk_high[:, g, :], tokens, start=True, stop=False)
                nc.tensor.matmul(front[:, QK_BANK, :], wqk_low[:, g, :], tokens, start=False,
                                 stop=True).then_inc(qk_ready, 1)

            def project_vr(c, u):
                pe.wait_ge(xt_copied, c + 1)
                for n in range(NU):
                    last = nc.tensor.matmul(front[:, u, n * VR:(n + 1) * VR], xt[:, u * NU + n, :].bitcast(F32),
                                            wvr[:, :], start=True, stop=True)
                last.then_inc(vr_ready, 1)

            def scores(c, u, par, first):
                if not first:
                    pe.wait_ge(shift_done, 2 * (c - 1) + u + 1)
                for n in range(NU):
                    last = nc.tensor.matmul(score[u][:, n * P:(n + 1) * P],
                                            q_t[par][:, u * NU + n, :, :].rearrange("k g q -> k (g q)"),
                                            k_t[par][:, u * NU + n, :, :].rearrange("k h q -> k (h q)"),
                                            start=True, stop=True)
                last.then_inc(scores_ready, 1)

            def turn_probs(c, u, first):
                pe.wait_ge(exp_done, 2 * c + u + 1)
                if not first or u == 1:
                    pe.wait_ge(probs_t_copied, 2 * c + u)
                for n in range(NU):
                    last = nc.tensor.transpose(turned[:, n * P:(n + 1) * P], probs[u][:, n, :], ident[:, :])
                last.then_inc(probs_turned, 1)

            def attend(c, par, early):
                pe.wait_ge(probs_t_copied, 2 * c + 2)
                pe.wait_ge(v_copied_act, c + 1)
                pe.wait_ge(v_copied_dve, c + 1)
                if not early:
                    pe.wait_ge(attn_normed, c)
                pe.nop(nofuse=True)
                for u in range(U):
                    for n in range(NU):
                        for g in range(G):
                            last = nc.tensor.matmul(attn_ps[g * F:(g + 1) * F, u, n * H * VW:(n + 1) * H * VW],
                                                    probs_t[par][:, u * NU + n, g, :],
                                                    v[par][:, u * NU + n, g, :, :].rearrange("p h d -> p (h d)"),
                                                    start=True, stop=True)
                last.then_inc(attn_ready, 1)

            def step(c, par, kind):
                first, last, early = kind == "first", kind == "last", kind == "second"
                nxt = 1 - par
                pe.wait_ge(qk_copied, 2 * c + 2)
                scores(c, 0, par, first)
                if not last:
                    project_qk(c + 1, 0, False)
                scores(c, 1, par, first)
                if not last:
                    project_vr(c + 1, 0)
                    project_vr(c + 1, 1)
                    project_qk(c + 1, 1, False)
                turn_probs(c, 0, first)
                if not first:
                    attend(c - 1, nxt, early)
                if kind not in ("next_to_last", "last"):
                    turn_x(c + 2, par, False)
                turn_probs(c, 1, first)

            turn_x(0, 0, True)
            project_qk(0, 0, True)
            project_qk(0, 1, False)
            project_vr(0, 0)
            project_vr(0, 1)
            turn_x(1, 1, False)
            step(0, 0, "first")
            step(1, 1, "second")
            with pe.Fori(0, n_chunks // UNROLL - 1) as i:
                for k in range(2, 2 + UNROLL):
                    step(UNROLL * i + k, k % 2, "middle")
            step(n_chunks - 2, 0, "next_to_last")
            step(n_chunks - 1, 1, "last")
            attend(n_chunks - 1, 1, False)


_INS = ["r_input_emb", "L0_rec_QW", "L0_rec_Qb", "L0_rec_KW", "L0_rec_Kb", "L0_rec_VW", "L0_rec_Vb", "L0_rec_RW",
        "L0_rec_Rb", "L0_rec_gamma", "L0_rec_beta"]


def kernel(**inputs):
    import numpy as _np
    import concourse.bacc as _bacc
    from concourse import mybir as _mybir
    from concourse.bass_utils import run_bass_kernel_spmd as _run

    nc = _bacc.Bacc("TRN2", target_bir_lowering=False, num_devices=1)
    arrays, args = {}, []
    for name in _INS:
        a = _np.ascontiguousarray(inputs[name])
        arrays[f"in_{name}_dram"] = a
        args.append(nc.dram_tensor(f"in_{name}_dram", a.shape, _mybir.dt.from_np(a.dtype), kind="ExternalInput").ap())
    out = nc.dram_tensor("out_0_dram", arrays["in_r_input_emb_dram"].shape, _mybir.dt.float32, kind="ExternalOutput").ap()
    rec_attention(nc, *args, out)
    r = _run(nc, [arrays], core_ids=[0])
    return r.results[0]["out_0_dram"]
```
